# Optimizing a Trainium2 kernel written in Bass

```python
import numpy as np
import jax
import jax.numpy as jnp

def _softmax(x, axis=-1):
    return jax.nn.softmax(x, axis=axis)

def _gelu(x):
    return jax.nn.gelu(x, approximate=True)

def _silu(x):
    return jax.nn.silu(x)

def _sigmoid(x):
    return jax.nn.sigmoid(x)

def _layernorm(x, axis=-1, eps=1e-05):
    m = jnp.mean(x, axis=axis, keepdims=True)
    v = jnp.var(x, axis=axis, keepdims=True)
    return (x - m) / jnp.sqrt(v + eps)

def _scatter_add(tgt, idx, src, axis=0):
    return tgt.at[idx].add(src)

def _segment_sum(src, seg, n):
    return jax.ops.segment_sum(src, seg, n)
kernel_name = 'mk_dlrm_tower_d1_rec_r8_065ea2'

def setup_inputs(seed: int=0):
    np.random.seed(seed)
    _w = jnp.asarray

    def _rec_inputs():
        import jax
        import jax.numpy as jnp
        _tk = jax.random.key(seed)
        ids = jnp.stack([jax.random.randint(jax.random.fold_in(_tk, 200 + f), (512,), 0, v, jnp.int32) for f, v in enumerate([1000, 1250, 1250, 125000, 1000, 12500, 12500, 1250, 12500, 12500, 1000, 1250, 1000, 1250, 12500, 12500, 1250, 1000, 1250, 1000, 12500, 12500, 1250, 1000, 1250, 1000])], axis=1)
        tbl_0 = 0.05 * jax.random.normal(jax.random.fold_in(_tk, 500 + 0), (1000, 128), jnp.float32)
        tbl_1 = 0.05 * jax.random.normal(jax.random.fold_in(_tk, 500 + 1), (1250, 128), jnp.float32)
        tbl_2 = 0.05 * jax.random.normal(jax.random.fold_in(_tk, 500 + 2), (1250, 128), jnp.float32)
        tbl_3 = 0.05 * jax.random.normal(jax.random.fold_in(_tk, 500 + 3), (125000, 128), jnp.float32)
        tbl_4 = 0.05 * jax.random.normal(jax.random.fold_in(_tk, 500 + 4), (1000, 128), jnp.float32)
        tbl_5 = 0.05 * jax.random.normal(jax.random.fold_in(_tk, 500 + 5), (12500, 128), jnp.float32)
        tbl_6 = 0.05 * jax.random.normal(jax.random.fold_in(_tk, 500 + 6), (12500, 128), jnp.float32)
        tbl_7 = 0.05 * jax.random.normal(jax.random.fold_in(_tk, 500 + 7), (1250, 128), jnp.float32)
        tbl_8 = 0.05 * jax.random.normal(jax.random.fold_in(_tk, 500 + 8), (12500, 128), jnp.float32)
        tbl_9 = 0.05 * jax.random.normal(jax.random.fold_in(_tk, 500 + 9), (12500, 128), jnp.float32)
        tbl_10 = 0.05 * jax.random.normal(jax.random.fold_in(_tk, 500 + 10), (1000, 128), jnp.float32)
        tbl_11 = 0.05 * jax.random.normal(jax.random.fold_in(_tk, 500 + 11), (1250, 128), jnp.float32)
        tbl_12 = 0.05 * jax.random.normal(jax.random.fold_in(_tk, 500 + 12), (1000, 128), jnp.float32)
        tbl_13 = 0.05 * jax.random.normal(jax.random.fold_in(_tk, 500 + 13), (1250, 128), jnp.float32)
        tbl_14 = 0.05 * jax.random.normal(jax.random.fold_in(_tk, 500 + 14), (12500, 128), jnp.float32)
        tbl_15 = 0.05 * jax.random.normal(jax.random.fold_in(_tk, 500 + 15), (12500, 128), jnp.float32)
        tbl_16 = 0.05 * jax.random.normal(jax.random.fold_in(_tk, 500 + 16), (1250, 128), jnp.float32)
        tbl_17 = 0.05 * jax.random.normal(jax.random.fold_in(_tk, 500 + 17), (1000, 128), jnp.float32)
        tbl_18 = 0.05 * jax.random.normal(jax.random.fold_in(_tk, 500 + 18), (1250, 128), jnp.float32)
        tbl_19 = 0.05 * jax.random.normal(jax.random.fold_in(_tk, 500 + 19), (1000, 128), jnp.float32)
        tbl_20 = 0.05 * jax.random.normal(jax.random.fold_in(_tk, 500 + 20), (12500, 128), jnp.float32)
        tbl_21 = 0.05 * jax.random.normal(jax.random.fold_in(_tk, 500 + 21), (12500, 128), jnp.float32)
        tbl_22 = 0.05 * jax.random.normal(jax.random.fold_in(_tk, 500 + 22), (1250, 128), jnp.float32)
        tbl_23 = 0.05 * jax.random.normal(jax.random.fold_in(_tk, 500 + 23), (1000, 128), jnp.float32)
        tbl_24 = 0.05 * jax.random.normal(jax.random.fold_in(_tk, 500 + 24), (1250, 128), jnp.float32)
        tbl_25 = 0.05 * jax.random.normal(jax.random.fold_in(_tk, 500 + 25), (1000, 128), jnp.float32)
        _rk = jax.random.fold_in(_tk, 7)
        r_bottom_output = -0.000520686 + 1.00062 * jax.random.normal(jax.random.fold_in(_rk, 101), (512, 128), jnp.float32)
        W_top1 = 0.0456912 * jax.random.normal(jax.random.fold_in(_tk, 801), (479, 512), jnp.float32)
        W_top2 = 0.0441942 * jax.random.normal(jax.random.fold_in(_tk, 802), (512, 256), jnp.float32)
        W_top3 = 0.0625 * jax.random.normal(jax.random.fold_in(_tk, 803), (256, 1), jnp.float32)
        b_top1 = jnp.zeros((512,), jnp.float32)
        b_top2 = jnp.zeros((256,), jnp.float32)
        return (r_bottom_output, ids, tbl_0, tbl_1, tbl_2, tbl_3, tbl_4, tbl_5, tbl_6, tbl_7, tbl_8, tbl_9, tbl_10, tbl_11, tbl_12, tbl_13, tbl_14, tbl_15, tbl_16, tbl_17, tbl_18, tbl_19, tbl_20, tbl_21, tbl_22, tbl_23, tbl_24, tbl_25, W_top1, b_top1, W_top2, b_top2, W_top3)
    r_bottom_output, ids, tbl_0, tbl_1, tbl_2, tbl_3, tbl_4, tbl_5, tbl_6, tbl_7, tbl_8, tbl_9, tbl_10, tbl_11, tbl_12, tbl_13, tbl_14, tbl_15, tbl_16, tbl_17, tbl_18, tbl_19, tbl_20, tbl_21, tbl_22, tbl_23, tbl_24, tbl_25, W_top1, b_top1, W_top2, b_top2, W_top3 = _rec_inputs()

    def _L0_rec_setup():
        import jax, jax.numpy as jnp
        import numpy as np
        NUM_FEATURES = 27
        _TRIU_I, _TRIU_J = np.triu_indices(NUM_FEATURES, k=1)
        key = jax.random.key(seed)
        k1, k2 = jax.random.split(key)
        bottom_output = jax.random.normal(k1, (2048, 128), dtype=jnp.float32)
        embeddings = jax.random.normal(k2, (2048, 26, 128), dtype=jnp.float32)
        return {'bottom_output': bottom_output, 'embeddings': embeddings}
    _L0_rec_all = _L0_rec_setup()
    _L0_rec_in = {k: v for k, v in _L0_rec_all.items() if k in ()}
    del _L0_rec_all
    return {'r_bottom_output': r_bottom_output, 'ids': ids, 'tbl_0': tbl_0, 'tbl_1': tbl_1, 'tbl_2': tbl_2, 'tbl_3': tbl_3, 'tbl_4': tbl_4, 'tbl_5': tbl_5, 'tbl_6': tbl_6, 'tbl_7': tbl_7, 'tbl_8': tbl_8, 'tbl_9': tbl_9, 'tbl_10': tbl_10, 'tbl_11': tbl_11, 'tbl_12': tbl_12, 'tbl_13': tbl_13, 'tbl_14': tbl_14, 'tbl_15': tbl_15, 'tbl_16': tbl_16, 'tbl_17': tbl_17, 'tbl_18': tbl_18, 'tbl_19': tbl_19, 'tbl_20': tbl_20, 'tbl_21': tbl_21, 'tbl_22': tbl_22, 'tbl_23': tbl_23, 'tbl_24': tbl_24, 'tbl_25': tbl_25, 'W_top1': W_top1, 'b_top1': b_top1, 'W_top2': W_top2, 'b_top2': b_top2, 'W_top3': W_top3}

def reference(r_bottom_output, ids, tbl_0, tbl_1, tbl_2, tbl_3, tbl_4, tbl_5, tbl_6, tbl_7, tbl_8, tbl_9, tbl_10, tbl_11, tbl_12, tbl_13, tbl_14, tbl_15, tbl_16, tbl_17, tbl_18, tbl_19, tbl_20, tbl_21, tbl_22, tbl_23, tbl_24, tbl_25, W_top1, b_top1, W_top2, b_top2, W_top3):
    import jax
    import jax.numpy as jnp

    def _L0_rec_ref(bottom_output, embeddings):
        import jax, jax.numpy as jnp
        import numpy as np
        NUM_FEATURES = 27
        _TRIU_I, _TRIU_J = np.triu_indices(NUM_FEATURES, k=1)
        all_emb = jnp.concatenate([bottom_output[:, None, :], embeddings], axis=1)
        gram = jnp.einsum('bfd,bgd->bfg', all_emb, all_emb)
        return gram[:, _TRIU_I, _TRIU_J]
    e = jnp.stack([tbl_0[ids[:, 0]], tbl_1[ids[:, 1]], tbl_2[ids[:, 2]], tbl_3[ids[:, 3]], tbl_4[ids[:, 4]], tbl_5[ids[:, 5]], tbl_6[ids[:, 6]], tbl_7[ids[:, 7]], tbl_8[ids[:, 8]], tbl_9[ids[:, 9]], tbl_10[ids[:, 10]], tbl_11[ids[:, 11]], tbl_12[ids[:, 12]], tbl_13[ids[:, 13]], tbl_14[ids[:, 14]], tbl_15[ids[:, 15]], tbl_16[ids[:, 16]], tbl_17[ids[:, 17]], tbl_18[ids[:, 18]], tbl_19[ids[:, 19]], tbl_20[ids[:, 20]], tbl_21[ids[:, 21]], tbl_22[ids[:, 22]], tbl_23[ids[:, 23]], tbl_24[ids[:, 24]], tbl_25[ids[:, 25]]], axis=1)
    z = _L0_rec_ref(r_bottom_output, e)
    z = z.reshape(z.shape[0], -1)
    h = jnp.concatenate([z, r_bottom_output], axis=1)
    h = jnp.maximum(h @ W_top1 + b_top1, 0.0)
    h = jnp.maximum(h @ W_top2 + b_top2, 0.0)
    y = h @ W_top3
    return y

_drawn_inputs = setup_inputs


def setup_inputs(seed=0):
    import zlib

    import numpy as np

    out = dict(_drawn_inputs(seed))
    spreads = {'b_top1': (0.0, 0.1), 'b_top2': (0.0, 0.1)}
    factors = {}
    for name, (base, spread) in spreads.items():
        noise = np.random.default_rng([zlib.crc32(name.encode()), seed]).standard_normal(out[name].shape)
        drawn = base * np.exp(spread * noise) if base else spread * noise
        out[name] = jnp.asarray(drawn.astype(out[name].dtype))
    for name, factor in factors.items():
        out[name] = (out[name] * factor).astype(out[name].dtype)
    return out
```

```python
import concourse.bass as bass
from concourse import mybir
from contextlib import ExitStack

P = 128
D = 128
F = 27
SLOTS = 32
COLS = 28
Q = 4
JQ = COLS // Q


def slot_order(looked):
    return [1 + k for k in looked] + [0] + [1 + k for k in range(F - 1) if k not in looked]


def dlrm_tower(nc, bottom, ids_rows, ids_cols, tables, looked, w_pair, w_bottom, b_top1, w_top2,
               b_top2, w_top3, out):
    f32, f32r, i32 = mybir.dt.float32, mybir.dt.float32r, mybir.dt.int32
    ALU, ACT = mybir.AluOpType, mybir.ActivationFunctionType

    B = bottom.shape[0] * bottom.shape[1]
    T = B // P
    gathered = [k for k in range(F - 1) if k not in looked]
    L, K = len(looked), len(gathered)
    VROWS = tables[looked[0]].shape[0] if L else 0
    CH = 8
    VP = VROWS // CH
    VP16 = VP // 16 * 16
    N1, N2 = b_top1.shape[1], b_top2.shape[1]
    NB = 4
    units = [list(range(a, min(a + NB, K))) for a in range(0, K, NB)]
    U = len(units)
    GH = 16
    HALVES = P // Q // GH
    MU = N1 + N2 + 1

    ctx = ExitStack()
    with ctx:
        def sb(name, shape, dt=f32):
            return ctx.enter_context(nc.sbuf_tensor(name, shape, dt))

        def pb(name, cols):
            return ctx.enter_context(nc.psum_tensor(name, [P, cols], f32))

        def sem(name):
            return ctx.enter_context(nc.semaphore(name))

        ids_g = sb("ids_g", [P, T, K], i32)
        ids_l = sb("ids_l", [VP, L, B], i32)
        rows_i = sb("rows_i", [P, CH], i32)
        rows_f = sb("rows_f", [P, CH])
        raw = sb("raw", [VP, L, CH, D])
        high = sb("high", [VP, 2, CH, D], f32r)
        low = sb("low", [VP, 2, CH, D], f32r)
        hot = sb("hot", [VP, CH, B], f32r)
        bot = sb("bot", [P, T, D])
        bot_t = sb("bot_t", [D, B])
        emb = sb("emb", [P, 2, K, D])
        feat = sb("feat", [D, B, SLOTS])
        pairs = sb("pairs", [P, 2, JQ, P])
        ident = sb("ident", [P, P])
        wp = sb("wp", [P, JQ, N1, P])
        wb = sb("wb", [P, N1, P])
        w2 = sb("w2", [P, N1, N2, P])
        w3 = sb("w3", [P, N2])
        b1 = sb("b1", [P, N1])
        b2 = sb("b2", [P, N2])
        h1 = sb("h1", [P, N1, P])
        h2 = sb("h2", [P, N2, P])
        y = sb("y", [1, B])

        gram = pb("gram", GH * P)
        turned = [pb("turned0", 512), pb("turned1", 512)]
        layer = [pb("layer0", 512), pb("layer1", 512)]

        ids_g_in = sem("ids_g_in")
        ids_l_in = sem("ids_l_in")
        bot_in = sem("bot_in")
        raw_in = [sem(f"raw_in{n}") for n in range(L)]
        w1_in = sem("w1_in")
        w2_in = sem("w2_in")
        emb_in = [[sem(f"emb_in{t}_{u}") for u in range(U)] for t in range(T)]
        zeroed = sem("zeroed")
        ident_ok = sem("ident_ok")
        rows_ok = sem("rows_ok")
        rows_f_ok = sem("rows_f_ok")
        pads_ok = sem("pads_ok")
        high_ok = sem("high_ok")
        low_ok = sem("low_ok")
        hot_ok = sem("hot_ok")
        hot_used = sem("hot_used")
        turned_ok = sem("turned_ok")
        feat_act = sem("feat_act")
        feat_dve = sem("feat_dve")
        bot_t_ok = sem("bot_t_ok")
        gram_ok = sem("gram_ok")
        pairs_act = sem("pairs_act")
        pairs_dve = sem("pairs_dve")
        layer_ok = sem("layer_ok")
        layer_out = sem("layer_out")
        y_out = sem("y_out")

        def unit_of(t, u):
            return 1 + L + t * U + u

        def wait_feat(eng, n):
            eng.wait_ge(feat_act, (n + 1) // 2)
            if n // 2:
                eng.wait_ge(feat_dve, n // 2)

        def wait_bank(eng, n):
            if n >= 2:
                eng.wait_ge(feat_dve if n % 2 else feat_act, n // 2)

        def move_unit(copy, n):
            src = turned[n % 2]
            if n <= L:
                slot = L if n == 0 else n - 1
                return copy(feat[:, :, slot], src[:, 0:B])
            t, u = divmod(n - 1 - L, U)
            k = units[u]
            slots = slice(L + 1 + k[0], L + 2 + k[-1])
            return copy(feat[:, t * P:(t + 1) * P, slots],
                        src[:, 0:len(k) * P].rearrange("d (k b) -> d b k", b=P))

        def move_pairs(copy, t, half, s):
            rows = slice(32 * s, 32 * s + 32)
            for q in range(Q):
                src = gram[rows, :].rearrange("p (g c) -> p c g", c=P)
                last = copy(pairs[32 * q:32 * q + 32, t % 2, :, Q * GH * half + s:Q * GH * (half + 1):Q],
                            src[:, COLS * s + q:COLS * (s + 1):Q, :])
            return last

        block = ctx.enter_context(nc.Block())

        @block.sync
        def _(sp):
            sp.dma_start(ids_g[:], ids_rows).then_inc(ids_g_in, 16)
            sp.dma_start(bot[:], bottom.rearrange("t p d -> p t d")).then_inc(bot_in, 16)
            if L:
                sp.dma_start(ids_l[:], ids_cols.rearrange("(o l) b -> o l b", o=1).to_broadcast([VP, L, B])
                             ).then_inc(ids_l_in, 16)
            for n, k in enumerate(looked):
                rows = tables[k].rearrange("(p c) d -> p c d", c=CH)
                sp.dma_start(raw[0:VP16, n], rows[0:VP16]).then_inc(raw_in[n], 16)
                sp.dma_start(raw[VP16:VP, n], rows[VP16:VP]).then_inc(raw_in[n], 16)
            sp.dma_start(wb[:], w_bottom.rearrange("p (n m) -> p n m", n=N1)).then_inc(w1_in, 16)
            sp.dma_start(wp[:], w_pair.rearrange("p j (n m) -> p j n m", n=N1)).then_inc(w1_in, 16)
            sp.dma_start(b1[:], b_top1).then_inc(w1_in, 16)
            sp.dma_start(w2[:], w_top2.rearrange("(k p) (n m) -> p k n m", p=P, n=N2)).then_inc(w2_in, 16)
            sp.dma_start(b2[:], b_top2).then_inc(w2_in, 16)
            sp.dma_start(w3[:], w_top3).then_inc(w2_in, 16)
            sp.wait_ge(layer_out, T * MU)
            sp.dma_start(out, y[:]).then_inc(y_out, 16)
            sp.wait_ge(y_out, 16)

        @block.gpsimd
        def _(pool):
            nc.gpsimd.memset(ident[:], 0.0).then_inc(zeroed, 1)
            nc.gpsimd.iota(rows_i[:], [[1, CH]], base=0, channel_multiplier=CH).then_inc(rows_ok, 1)
            pool.wait_ge(zeroed, 1)
            nc.gpsimd.affine_select(out=ident[:], in_=ident[:], compare_op=ALU.not_equal, fill=1.0,
                                    base=0, pattern=[[-1, P]], channel_multiplier=1).then_inc(ident_ok, 1)
            pool.wait_ge(ids_g_in, 16)
            for t in range(T):
                for u, ks in enumerate(units):
                    if t >= 2:
                        pool.wait_ge(turned_ok, unit_of(t - 2, u) + 1)
                    for k in ks:
                        nc.gpsimd.indirect_dma_start(
                            out=emb[:, t % 2, k, :], out_offset=None, in_=tables[gathered[k]],
                            in_offset=bass.IndirectOffsetOnAxis(ap=ids_g[:, t, k:k + 1], axis=0),
                        ).then_inc(emb_in[t][u], 16)

        @block.vector
        def _(dve):
            copy = nc.vector.tensor_copy

            def spread(n):
                dve.wait_ge(high_ok, n + 1)
                if n >= 2:
                    dve.wait_ge(hot_used, CH * (n - 1))
                nc.vector.tensor_tensor(low[:, n % 2], raw[:, n], high[:, n % 2].bitcast(f32),
                                        ALU.subtract).then_inc(low_ok, 1)
                for c in range(CH):
                    if n >= 1:
                        dve.wait_ge(hot_used, CH * (n - 1) + c + 1)
                    nc.vector.tensor_scalar(hot[:, c], ids_l[:, n], rows_f[0:VP, c:c + 1], None,
                                            ALU.is_equal).then_inc(hot_ok, 1)

            def unit(n):
                if n % 2:
                    dve.wait_ge(turned_ok, n + 1)
                    move_unit(copy, n).then_inc(feat_dve, 1)

            dve.wait_ge(rows_ok, 1)
            copy(rows_f[:], rows_i[:]).then_inc(rows_f_ok, 1)
            nc.vector.memset(feat[:, :, F:SLOTS], 0.0).then_inc(pads_ok, 1)
            if L:
                dve.wait_ge(ids_l_in, 16)
                dve.wait_ge(rows_f_ok, 1)
            for n in range(L):
                spread(n)
                unit(n)
            unit(L)
            for t in range(T):
                for u in range(U):
                    unit(unit_of(t, u))
                for half in range(HALVES):
                    dve.wait_ge(gram_ok, HALVES * t + half + 1)
                    if t >= 2 and half == 0:
                        dve.wait_ge(layer_ok, MU * (t - 2) + N1)
                    move_pairs(copy, t, half, 2)
                    move_pairs(copy, t, half, 3).then_inc(pairs_dve, 1)

        @block.scalar
        def _(act):
            copy = nc.scalar.copy

            def split(n):
                act.wait_ge(raw_in[n], 32)
                if n >= 2:
                    act.wait_ge(hot_used, CH * (n - 1))
                copy(high[:, n % 2], raw[:, n]).then_inc(high_ok, 1)

            def unit(n):
                if n % 2 == 0:
                    act.wait_ge(turned_ok, n + 1)
                    move_unit(copy, n).then_inc(feat_act, 1)

            def relu(t, m):
                act.wait_ge(layer_ok, MU * t + m + 1)
                src = layer[(MU * t + m) % 2]
                if m < N1:
                    if t == 0 and m == 0:
                        act.wait_ge(w1_in, 48)
                    ins = nc.scalar.activation(h1[:, m], src[:, 0:P], ACT.Relu, bias=b1[:, m:m + 1])
                elif m < N1 + N2:
                    if t == 0 and m == N1:
                        act.wait_ge(w2_in, 48)
                    n = m - N1
                    ins = nc.scalar.activation(h2[:, n], src[:, 0:P], ACT.Relu, bias=b2[:, n:n + 1])
                else:
                    ins = copy(y[0:1, t * P:(t + 1) * P], src[0:1, 0:P])
                ins.then_inc(layer_out, 1)

            for n in range(min(2, L)):
                split(n)
            act.wait_ge(turned_ok, 1)
            copy(bot_t[:], turned[0][:, 0:B]).then_inc(bot_t_ok, 1)
            unit(0)
            for n in range(L):
                if n + 2 < L:
                    split(n + 2)
                unit(n + 1)
            for t in range(T):
                for u in range(U):
                    unit(unit_of(t, u))
                    if t and u < N1:
                        relu(t - 1, u)
                for half in range(HALVES):
                    act.wait_ge(gram_ok, HALVES * t + half + 1)
                    if t >= 2 and half == 0:
                        act.wait_ge(layer_ok, MU * (t - 2) + N1)
                    move_pairs(copy, t, half, 0)
                    move_pairs(copy, t, half, 1).then_inc(pairs_act, 1)
                    if t and half == 0:
                        for m in range(N1, MU):
                            relu(t - 1, m)
            for m in range(MU):
                relu(T - 1, m)

        @block.tensor
        def _(pe):
            groups = feat[:].rearrange("d (t g s) f -> d t g (s f)", t=T, s=Q)

            def lookup(n):
                wait_bank(pe, n + 1)
                pe.wait_ge(low_ok, n + 1)
                for c in range(CH):
                    pe.wait_ge(hot_ok, CH * n + c + 1)
                    nc.tensor.matmul(turned[(n + 1) % 2][:, 0:B], high[:, n % 2, c], hot[:, c],
                                     start=(c == 0), stop=False)
                    last = nc.tensor.matmul(turned[(n + 1) % 2][:, 0:B], low[:, n % 2, c], hot[:, c],
                                            start=False, stop=(c == CH - 1))
                    if c < CH - 1:
                        last.then_inc(hot_used, 1)
                last.then_inc(hot_used, 1)
                pe.wait_ge(hot_used, CH * (n + 1))
                pe.sem_inc(turned_ok, 1)

            def turn(t, u):
                n = unit_of(t, u)
                wait_bank(pe, n)
                pe.wait_ge(emb_in[t][u], 16 * len(units[u]))
                for i, k in enumerate(units[u]):
                    last = nc.tensor.transpose(turned[n % 2][:, i * P:(i + 1) * P], emb[:, t % 2, k], ident[:])
                last.then_inc(turned_ok, 1)

            def multiply(t, half):
                n = HALVES * t + half
                if n:
                    pe.wait_ge(pairs_act, n)
                    pe.wait_ge(pairs_dve, n)
                for i in range(GH):
                    g = GH * half + i
                    last = nc.tensor.matmul(gram[:, i * P:i * P + Q * COLS], groups[:, t, g],
                                            groups[:, t, g].rearrange("d (s f) -> d s f", s=Q)[:, :, 0:COLS], start=True, stop=True)
                last.then_inc(gram_ok, 1)

            def dense(t, m):
                n = MU * t + m
                if n >= 2:
                    pe.wait_ge(layer_out, n - 1)
                dst = layer[n % 2]
                if m < N1:
                    if m == 0:
                        if t == 0:
                            pe.wait_ge(w1_in, 48)
                            pe.wait_ge(bot_t_ok, 1)
                        pe.wait_ge(pairs_act, HALVES * (t + 1))
                        pe.wait_ge(pairs_dve, HALVES * (t + 1))
                    nc.tensor.matmul(dst[:, 0:P], wb[:, m], bot_t[:, t * P:(t + 1) * P], start=True, stop=False)
                    for j in range(JQ):
                        last = nc.tensor.matmul(dst[:, 0:P], wp[:, j, m], pairs[:, t % 2, j],
                                                start=False, stop=(j == JQ - 1))
                elif m < N1 + N2:
                    if t == 0:
                        pe.wait_ge(w2_in, 48)
                    pe.wait_ge(layer_out, MU * t + N1)
                    for k in range(N1):
                        last = nc.tensor.matmul(dst[:, 0:P], w2[:, k, m - N1], h1[:, k],
                                                start=(k == 0), stop=(k == N1 - 1))
                else:
                    pe.wait_ge(layer_out, MU * t + N1 + N2)
                    for k in range(N2):
                        last = nc.tensor.matmul(dst[0:1, 0:P], w3[:, k:k + 1], h2[:, k],
                                                start=(k == 0), stop=(k == N2 - 1))
                last.then_inc(layer_ok, 1)

            pe.wait_ge(ident_ok, 1)
            pe.wait_ge(bot_in, 16)
            for t in range(T):
                last = nc.tensor.transpose(turned[0][:, t * P:(t + 1) * P], bot[:, t], ident[:])
            last.then_inc(turned_ok, 1)
            for n in range(L):
                lookup(n)
            pe.wait_ge(pads_ok, 1)
            for t in range(T):
                for u in range(U):
                    turn(t, u)
                    if t and u < N1:
                        dense(t - 1, u)
                wait_feat(pe, unit_of(t, U - 1) + 1)
                for half in range(HALVES):
                    multiply(t, half)
                    if t and half == 0:
                        for m in range(N1, MU):
                            dense(t - 1, m)
            for m in range(MU):
                dense(T - 1, m)


LOOKED = 6


def kernel(**inputs):
    import numpy as np
    import concourse.bacc as bacc
    from concourse.bass_utils import run_bass_kernel_spmd

    tables = [np.asarray(inputs[f"tbl_{k}"]) for k in range(F - 1)]
    least = min(t.shape[0] for t in tables)
    small = [k for k in range(F - 1) if tables[k].shape[0] == least and least % 8 == 0 and least <= 8 * P]
    looked = small[:LOOKED]
    order = slot_order(looked)

    ids = np.asarray(inputs["ids"])
    bottom = np.asarray(inputs["r_bottom_output"])
    B = ids.shape[0]
    T = B // P
    gathered = [k for k in range(F - 1) if k not in looked]
    ids_rows = ids[:, gathered].reshape(T, P, -1).transpose(1, 0, 2)
    ids_cols = ids[:, looked].T

    w1 = np.asarray(inputs["W_top1"])
    pair_rows = F * (F - 1) // 2
    w_pair = np.zeros((P, JQ, w1.shape[1]), w1.dtype)
    at = {pair: n for n, pair in enumerate((i, j) for i in range(F) for j in range(i + 1, F))}
    for high in range(F):
        for low in range(high):
            pair = tuple(sorted((order[low], order[high])))
            w_pair[32 * (high % Q) + low, high // Q] = w1[at[pair]]

    arrays = {
        "bottom": bottom.reshape(T, P, D),
        "ids_rows": ids_rows,
        "ids_cols": ids_cols,
        "w_pair": w_pair,
        "w_bottom": w1[pair_rows:],
        "b_top1": np.asarray(inputs["b_top1"]).reshape(-1, P).T,
        "w_top2": np.asarray(inputs["W_top2"]),
        "b_top2": np.asarray(inputs["b_top2"]).reshape(-1, P).T,
        "w_top3": np.asarray(inputs["W_top3"]).reshape(-1, P).T,
    }
    arrays |= {f"table{k}": t for k, t in enumerate(tables)}
    arrays = {n: np.ascontiguousarray(a) for n, a in arrays.items()}
    nc = bacc.Bacc("TRN2", target_bir_lowering=False, num_devices=1)
    aps = {n: nc.dram_tensor(n, a.shape, mybir.dt.from_np(a.dtype), kind="ExternalInput").ap()
           for n, a in arrays.items()}
    out = nc.dram_tensor("y_dram", (1, B), mybir.dt.float32, kind="ExternalOutput").ap()
    dlrm_tower(nc, aps["bottom"], aps["ids_rows"], aps["ids_cols"],
               [aps[f"table{k}"] for k in range(F - 1)], looked, aps["w_pair"], aps["w_bottom"],
               aps["b_top1"], aps["w_top2"], aps["b_top2"], aps["w_top3"], out)
    r = run_bass_kernel_spmd(nc, [arrays], core_ids=[0])
    return r.results[0]["y_dram"].reshape(B, 1)
```

```python
import concourse.bass as bass
from concourse import mybir
from contextlib import ExitStack

P = 128
D = 128
F = 27
SLOTS = 32
REPEATS = {27: 1, 28: 2}
USED = 29
Q = 4
CHUNKS = 6
FIRST_TURN = 1


def slot_order(looked):
    return [1 + k for k in looked] + [0] + [1 + k for k in range(F - 1) if k not in looked]


def first_column(q):
    return q if q != 2 else 6


def place(low, high):
    if high < 3:
        return 32 * low + {1: 27, 2: 28}[high], 0
    q = high % Q
    return 32 * q + low, 0 if high in (24, 25) else (high - first_column(q)) // Q


def dlrm_tower(nc, bottom, ids_rows, ids_cols, tables, looked, w_pair, w_bottom, b_top1, w_top2,
               b_top2, w_top3, out):
    f32, f32r, i32 = mybir.dt.float32, mybir.dt.float32r, mybir.dt.int32
    ALU, ACT = mybir.AluOpType, mybir.ActivationFunctionType

    B = bottom.shape[0] * bottom.shape[1]
    T = B // P
    gathered = [k for k in range(F - 1) if k not in looked]
    L, K = len(looked), len(gathered)
    VROWS = tables[looked[0]].shape[0] if L else 0
    CH = 8
    VP = VROWS // CH
    VP16 = VP // 16 * 16
    N1, N2 = b_top1.shape[1], b_top2.shape[1]
    NB = 4
    units = [list(range(a, min(a + NB, K))) for a in range(0, K, NB)]
    U = len(units)
    GH = 8
    PARTS = P // Q // GH
    MU = N1 + N2 + 1

    ctx = ExitStack()
    with ctx:
        def sb(name, shape, dt=f32):
            return ctx.enter_context(nc.sbuf_tensor(name, shape, dt))

        def pb(name, cols):
            return ctx.enter_context(nc.psum_tensor(name, [P, cols], f32))

        def sem(name):
            return ctx.enter_context(nc.semaphore(name))

        ids_g = sb("ids_g", [P, T, K], i32)
        ids_l = sb("ids_l", [P, L, B], i32)
        first_i = sb("first_i", [P, 1], i32)
        first_f = sb("first_f", [P, 1])
        ids_c = sb("ids_c", [P, 2, B], i32)
        raw = sb("raw", [VP, L, CH, D])
        high = sb("high", [VP, 2, CH, D], f32r)
        low = sb("low", [VP, 2, CH, D], f32r)
        hot = sb("hot", [VP, CH, B], f32r)
        bot = sb("bot", [P, T, D])
        bot_t = sb("bot_t", [D, B])
        emb = sb("emb", [P, 2, K, D])
        feat = sb("feat", [D, B, SLOTS])
        pairs = sb("pairs", [P, 2, CHUNKS, P])
        ident = sb("ident", [P, P])
        wp = sb("wp", [P, CHUNKS, N1, P])
        wb = sb("wb", [P, N1, P])
        w2 = sb("w2", [P, N1, N2, P])
        w3 = sb("w3", [P, N2])
        b1 = sb("b1", [P, N1])
        b2 = sb("b2", [P, N2])
        h1 = sb("h1", [P, N1, P])
        h2 = sb("h2", [P, N2, P])
        y = sb("y", [1, B])

        gram = [pb("gram0", GH * P), pb("gram1", GH * P)]
        turned = [pb("turned0", 512), pb("turned1", 512)]
        layer = [pb("layer0", 512), pb("layer1", 512)]

        ids_g_in = sem("ids_g_in")
        ids_l_in = [sem(f"ids_l_in{n}") for n in range(L)]
        bot_in = sem("bot_in")
        raw_in = [sem(f"raw_in{n}") for n in range(L)]
        w1_in = sem("w1_in")
        w2_in = sem("w2_in")
        emb_in = [[sem(f"emb_in{t}_{u}") for u in range(U)] for t in range(T)]
        zeroed = sem("zeroed")
        ident_ok = sem("ident_ok")
        first_ok = sem("first_ok")
        first_f_ok = sem("first_f_ok")
        ids_c_ok = sem("ids_c_ok")
        pads_ok = sem("pads_ok")
        high_ok = sem("high_ok")
        low_ok = sem("low_ok")
        hot_ok = sem("hot_ok")
        hot_used = sem("hot_used")
        turned_ok = sem("turned_ok")
        feat_act = sem("feat_act")
        feat_dve = sem("feat_dve")
        bot_t_ok = sem("bot_t_ok")
        gram_ok = sem("gram_ok")
        under_act = sem("under_act")
        under_dve = sem("under_dve")
        pairs_act = sem("pairs_act")
        pairs_dve = sem("pairs_dve")
        layer_ok = sem("layer_ok")
        layer_out = sem("layer_out")
        y_out = sem("y_out")

        fills = [("bottom",)]
        for n in range(L):
            fills.append(("lookup", n))
            if 0 <= n - FIRST_TURN < U:
                fills.append(("turn", 0, n - FIRST_TURN))
        head = len(fills)
        fills += [x for t in range(T) for u in range(U) if (x := ("turn", t, u)) not in fills]
        number = {x: n for n, x in enumerate(fills)}

        def by_act(n):
            return n < head or n % 2 == 0

        def wait_feat(eng, n):
            act = sum(by_act(m) for m in range(n))
            eng.wait_ge(feat_act, act)
            if n > act:
                eng.wait_ge(feat_dve, n - act)

        def wait_bank(eng, n):
            if n >= 2:
                same = sum(by_act(m) == by_act(n - 2) for m in range(n - 1))
                eng.wait_ge(feat_act if by_act(n - 2) else feat_dve, same)

        def wait_turned(eng, n):
            what, *at = fills[n]
            if what == "lookup":
                eng.wait_ge(hot_used, CH * (at[0] + 1))
            else:
                eng.wait_ge(turned_ok, sum(x[0] != "lookup" for x in fills[:n + 1]))

        def move_fill(copy, n):
            what, *at = fills[n]
            src = turned[n % 2]
            if what != "turn":
                slot = at[0] if what == "lookup" else L
                for again, first in REPEATS.items():
                    if slot == first:
                        copy(feat[:, :, again], src[:, 0:B])
                return copy(feat[:, :, slot], src[:, 0:B])
            t, u = at
            k = units[u]
            slots = slice(L + 1 + k[0], L + 2 + k[-1])
            return copy(feat[:, t * P:(t + 1) * P, slots],
                        src[:, 0:len(k) * P].rearrange("d (k b) -> d b k", b=P))

        def steps(t):
            turns = [("turn", t, u) for u in range(U) if number["turn", t, u] >= head]
            products = [("multiply", t, part) for part in range(PARTS)]
            if t == 0:
                return turns + products
            layers = [("dense", t - 1, m) for m in range(MU)]
            if t == T - 1:
                return turns[:-2] + layers[:N1 - 1] + turns[-2:-1] + layers[N1 - 1:] + turns[-1:] + products
            out, mixed = turns[:3], turns[3:]
            for i in range(N1 - 1):
                out.append(layers[i])
                out += mixed[i:i + 1]
            return (out + mixed[N1 - 1:] + products[:1] + layers[N1 - 1:N1] + products[1:2]
                    + layers[N1:MU - 1] + products[2:3] + layers[MU - 1:] + products[3:])

        def move_pairs(eng, copy, t, part, samples, under, done):
            src = gram[part % 2][:].rearrange("p (g c) -> p c g", c=P)

            def to(s):
                return slice(Q * GH * part + s, Q * GH * (part + 1), Q)

            for pair in ((0, 1), (2, 3)):
                for s in samples:
                    for q in pair:
                        a = F * s + first_column(q)
                        last = copy(pairs[32 * q:32 * q + 32, t % 2, :, to(s)],
                                    src[32 * s:32 * s + 32, a:a + Q * (CHUNKS - 1) + 1:Q])
                if pair == (0, 1):
                    last.then_inc(under, 1)
            eng.wait_ge(under, PARTS * t + part + 1)
            for s in samples:
                for q in range(2):
                    last = copy(pairs[32 * q:32 * q + 25, t % 2, 0, to(s)],
                                src[32 * s:32 * s + 25, F * s + 24 + q])
            last.then_inc(done, 1)

        ids_every = ids_cols.rearrange("(o l) b -> o l b", o=1).to_broadcast([P, L, B])

        block = ctx.enter_context(nc.Block())

        @block.sync
        def _(sp):
            sp.dma_start(ids_g[:], ids_rows).then_inc(ids_g_in, 16)
            for n, k in enumerate(looked):
                rows = tables[k].rearrange("(p c) d -> p c d", c=CH)
                sp.dma_start(raw[0:VP16, n], rows[0:VP16]).then_inc(raw_in[n], 16)
                sp.dma_start(raw[VP16:VP, n], rows[VP16:VP]).then_inc(raw_in[n], 16)
                if n + 2 < L:
                    sp.dma_start(ids_l[:, n + 2:n + 3], ids_every[:, n + 2:n + 3]).then_inc(ids_l_in[n + 2], 16)
            sp.dma_start(wb[:], w_bottom.rearrange("p (n m) -> p n m", n=N1)).then_inc(w1_in, 16)
            sp.dma_start(wp[:], w_pair.rearrange("p j (n m) -> p j n m", n=N1)).then_inc(w1_in, 16)
            sp.dma_start(b1[:], b_top1).then_inc(w1_in, 16)
            sp.dma_start(w2[:], w_top2.rearrange("(k p) (n m) -> p k n m", p=P, n=N2)).then_inc(w2_in, 16)
            sp.dma_start(b2[:], b_top2).then_inc(w2_in, 16)
            sp.dma_start(w3[:], w_top3).then_inc(w2_in, 16)
            sp.wait_ge(layer_out, T * MU)
            sp.dma_start(out, y[:]).then_inc(y_out, 16)
            sp.wait_ge(y_out, 16)

        @block.gpsimd
        def _(pool):
            nc.gpsimd.memset(ident[:], 0.0).then_inc(zeroed, 1)
            nc.gpsimd.iota(first_i[:], [[1, 1]], base=0, channel_multiplier=-CH).then_inc(first_ok, 1)
            pool.wait_ge(zeroed, 1)
            nc.gpsimd.affine_select(out=ident[:], in_=ident[:], compare_op=ALU.not_equal, fill=1.0,
                                    base=0, pattern=[[-1, P]], channel_multiplier=1).then_inc(ident_ok, 1)
            pool.wait_ge(ids_g_in, 16)
            for t in range(T):
                for u, ks in enumerate(units):
                    if t >= 2:
                        wait_turned(pool, number["turn", t - 2, u])
                    for k in ks:
                        nc.gpsimd.indirect_dma_start(
                            out=emb[:, t % 2, k, :], out_offset=None, in_=tables[gathered[k]],
                            in_offset=bass.IndirectOffsetOnAxis(ap=ids_g[:, t, k:k + 1], axis=0),
                        ).then_inc(emb_in[t][u], 16)

        @block.vector
        def _(dve):
            copy = nc.vector.tensor_copy

            def spread(n):
                dve.wait_ge(ids_c_ok, n + 1)
                for c in range(CH):
                    if n >= 1:
                        dve.wait_ge(hot_used, CH * (n - 1) + c + 1)
                    nc.vector.tensor_single_scalar(hot[:, c], ids_c[0:VP, n % 2], c,
                                                   ALU.is_equal).then_inc(hot_ok, 1)
                    if c == 1:
                        dve.wait_ge(high_ok, n + 1)
                        if n >= 2:
                            dve.wait_ge(hot_used, CH * (n - 1))
                        nc.vector.tensor_tensor(low[:, n % 2], raw[:, n], high[:, n % 2].bitcast(f32),
                                                ALU.subtract).then_inc(low_ok, 1)

            def fill(n):
                if not by_act(n):
                    wait_turned(dve, n)
                    move_fill(copy, n).then_inc(feat_dve, 1)

            dve.wait_ge(first_ok, 1)
            copy(first_f[:], first_i[:]).then_inc(first_f_ok, 1)
            nc.vector.memset(feat[:, :, USED:SLOTS], 0.0).then_inc(pads_ok, 1)
            for n in range(L):
                spread(n)
            for t in range(T):
                for what, *at in steps(t):
                    if what == "turn":
                        fill(number["turn", *at])
                    elif what == "multiply":
                        t, part = at
                        dve.wait_ge(gram_ok, PARTS * t + part + 1)
                        if t >= 2 and part == 0:
                            dve.wait_ge(layer_ok, MU * (t - 2) + N1)
                        move_pairs(dve, copy, t, part, (2, 3), under_dve, pairs_dve)

        @block.scalar
        def _(act):
            copy = nc.scalar.copy

            def split(n):
                act.wait_ge(ids_l_in[n], 16)
                if n == 0:
                    act.wait_ge(first_f_ok, 1)
                if n >= 2:
                    act.wait_ge(hot_ok, CH * (n - 1))
                nc.scalar.activation(ids_c[:, n % 2], ids_l[:, n], ACT.Identity,
                                     bias=first_f[:, 0:1]).then_inc(ids_c_ok, 1)
                act.wait_ge(raw_in[n], 32)
                if n >= 2:
                    act.wait_ge(hot_used, CH * (n - 1))
                copy(high[:, n % 2], raw[:, n]).then_inc(high_ok, 1)

            def fill(n):
                if by_act(n):
                    wait_turned(act, n)
                    move_fill(copy, n).then_inc(feat_act, 1)

            def relu(t, m):
                act.wait_ge(layer_ok, MU * t + m + 1)
                src = layer[(MU * t + m) % 2]
                if m < N1:
                    if t == 0 and m == 0:
                        act.wait_ge(w1_in, 48)
                    ins = nc.scalar.activation(h1[:, m], src[:, 0:P], ACT.Relu, bias=b1[:, m:m + 1])
                elif m < N1 + N2:
                    if t == 0 and m == N1:
                        act.wait_ge(w2_in, 48)
                    n = m - N1
                    ins = nc.scalar.activation(h2[:, n], src[:, 0:P], ACT.Relu, bias=b2[:, n:n + 1])
                else:
                    ins = copy(y[0:1, t * P:(t + 1) * P], src[0:1, 0:P])
                ins.then_inc(layer_out, 1)

            act.dma_start(ids_l[:, 0:1], ids_every[:, 0:1]).then_inc(ids_l_in[0], 16)
            act.dma_start(bot[:], bottom.rearrange("t p d -> p t d")).then_inc(bot_in, 16)
            act.dma_start(ids_l[:, 1:2], ids_every[:, 1:2]).then_inc(ids_l_in[1], 16)
            split(0)
            split(1)
            act.wait_ge(turned_ok, 1)
            copy(bot_t[:], turned[0][:, 0:B]).then_inc(bot_t_ok, 1)
            for n in range(head):
                fill(n)
                if fills[n][0] == "lookup" and fills[n][1] + 2 < L:
                    split(fills[n][1] + 2)
            for t in range(T):
                for what, *at in steps(t):
                    if what == "turn":
                        fill(number["turn", *at])
                    elif what == "dense":
                        relu(*at)
                    else:
                        t, part = at
                        act.wait_ge(gram_ok, PARTS * t + part + 1)
                        if t >= 2 and part == 0:
                            act.wait_ge(layer_ok, MU * (t - 2) + N1)
                        move_pairs(act, copy, t, part, (0, 1), under_act, pairs_act)
            for m in range(MU):
                relu(T - 1, m)

        @block.tensor
        def _(pe):
            groups = feat[:].rearrange("d (t g s) f -> d t g (s f)", t=T, s=Q)

            def lookup(n):
                m = number["lookup", n]
                wait_bank(pe, m)
                pe.wait_ge(high_ok, n + 1)
                for c in range(CH):
                    pe.wait_ge(hot_ok, CH * n + c + 1)
                    nc.tensor.matmul(turned[m % 2][:, 0:B], high[:, n % 2, c], hot[:, c],
                                     start=(c == 0), stop=False)
                    if c == 0:
                        pe.wait_ge(low_ok, n + 1)
                    nc.tensor.matmul(turned[m % 2][:, 0:B], low[:, n % 2, c], hot[:, c],
                                     start=False, stop=(c == CH - 1)).then_inc(hot_used, 1)

            def turn(t, u):
                n = number["turn", t, u]
                wait_bank(pe, n)
                pe.wait_ge(emb_in[t][u], 16 * len(units[u]))
                for i, k in enumerate(units[u]):
                    last = nc.tensor.transpose(turned[n % 2][:, i * P:(i + 1) * P], emb[:, t % 2, k], ident[:])
                last.then_inc(turned_ok, 1)

            def multiply(t, part):
                n = PARTS * t + part
                if n >= 2:
                    pe.wait_ge(pairs_act, n - 1)
                    pe.wait_ge(pairs_dve, n - 1)
                for i in range(GH):
                    g = GH * part + i
                    last = nc.tensor.matmul(gram[part % 2][:, i * P:i * P + Q * F], groups[:, t, g],
                                            groups[:, t, g].rearrange("d (s f) -> d s f", s=Q)[:, :, 0:F],
                                            start=True, stop=True)
                last.then_inc(gram_ok, 1)

            def dense(t, m):
                n = MU * t + m
                if n >= 2:
                    pe.wait_ge(layer_out, n - 1)
                dst = layer[n % 2]
                if m < N1:
                    if m == 0:
                        if t == 0:
                            pe.wait_ge(w1_in, 48)
                            pe.wait_ge(bot_t_ok, 1)
                    nc.tensor.matmul(dst[:, 0:P], wb[:, m], bot_t[:, t * P:(t + 1) * P], start=True, stop=False)
                    if m == 0:
                        pe.wait_ge(pairs_act, PARTS * (t + 1))
                        pe.wait_ge(pairs_dve, PARTS * (t + 1))
                    for j in range(CHUNKS):
                        last = nc.tensor.matmul(dst[:, 0:P], wp[:, j, m], pairs[:, t % 2, j],
                                                start=False, stop=(j == CHUNKS - 1))
                elif m < N1 + N2:
                    if t == 0:
                        pe.wait_ge(w2_in, 48)
                    for k in range(N1):
                        pe.wait_ge(layer_out, MU * t + k + 1)
                        last = nc.tensor.matmul(dst[:, 0:P], w2[:, k, m - N1], h1[:, k],
                                                start=(k == 0), stop=(k == N1 - 1))
                else:
                    for k in range(N2):
                        pe.wait_ge(layer_out, MU * t + N1 + k + 1)
                        last = nc.tensor.matmul(dst[0:1, 0:P], w3[:, k:k + 1], h2[:, k],
                                                start=(k == 0), stop=(k == N2 - 1))
                last.then_inc(layer_ok, 1)

            pe.wait_ge(ident_ok, 1)
            pe.wait_ge(bot_in, 16)
            for t in range(T):
                last = nc.tensor.transpose(turned[0][:, t * P:(t + 1) * P], bot[:, t], ident[:])
            last.then_inc(turned_ok, 1)
            for what, *at in fills[1:head]:
                (lookup if what == "lookup" else turn)(*at)
            pe.wait_ge(pads_ok, 1)
            for t in range(T):
                for what, *at in steps(t):
                    if what == "turn":
                        turn(*at)
                    elif what == "dense":
                        dense(*at)
                    else:
                        if at[1] == 0:
                            wait_feat(pe, max(head, number["turn", t, U - 1] + 1))
                        multiply(*at)
            for m in range(MU):
                dense(T - 1, m)


LOOKED = 6


def kernel(**inputs):
    import numpy as np
    import concourse.bacc as bacc
    from concourse.bass_utils import run_bass_kernel_spmd

    tables = [np.asarray(inputs[f"tbl_{k}"]) for k in range(F - 1)]
    least = min(t.shape[0] for t in tables)
    small = [k for k in range(F - 1) if tables[k].shape[0] == least and least % 8 == 0 and least <= 8 * P]
    looked = small[:LOOKED]
    order = slot_order(looked)

    ids = np.asarray(inputs["ids"])
    bottom = np.asarray(inputs["r_bottom_output"])
    B = ids.shape[0]
    T = B // P
    gathered = [k for k in range(F - 1) if k not in looked]
    ids_rows = ids[:, gathered].reshape(T, P, -1).transpose(1, 0, 2)
    ids_cols = ids[:, looked].T

    w1 = np.asarray(inputs["W_top1"])
    pair_rows = F * (F - 1) // 2
    w_pair = np.zeros((P, CHUNKS, w1.shape[1]), w1.dtype)
    at = {pair: n for n, pair in enumerate((i, j) for i in range(F) for j in range(i + 1, F))}
    for high in range(F):
        for low in range(high):
            w_pair[place(low, high)] = w1[at[tuple(sorted((order[low], order[high])))]]

    arrays = {
        "bottom": bottom.reshape(T, P, D),
        "ids_rows": ids_rows,
        "ids_cols": ids_cols,
        "w_pair": w_pair,
        "w_bottom": w1[pair_rows:],
        "b_top1": np.asarray(inputs["b_top1"]).reshape(-1, P).T,
        "w_top2": np.asarray(inputs["W_top2"]),
        "b_top2": np.asarray(inputs["b_top2"]).reshape(-1, P).T,
        "w_top3": np.asarray(inputs["W_top3"]).reshape(-1, P).T,
    }
    arrays |= {f"table{k}": t for k, t in enumerate(tables)}
    arrays = {n: np.ascontiguousarray(a) for n, a in arrays.items()}
    nc = bacc.Bacc("TRN2", target_bir_lowering=False, num_devices=1)
    aps = {n: nc.dram_tensor(n, a.shape, mybir.dt.from_np(a.dtype), kind="ExternalInput").ap()
           for n, a in arrays.items()}
    out = nc.dram_tensor("y_dram", (1, B), mybir.dt.float32, kind="ExternalOutput").ap()
    dlrm_tower(nc, aps["bottom"], aps["ids_rows"], aps["ids_cols"],
               [aps[f"table{k}"] for k in range(F - 1)], looked, aps["w_pair"], aps["w_bottom"],
               aps["b_top1"], aps["w_top2"], aps["b_top2"], aps["w_top3"], out)
    r = run_bass_kernel_spmd(nc, [arrays], core_ids=[0])
    return r.results[0]["y_dram"].reshape(B, 1)
```

```python
import concourse.bass as bass
from concourse import mybir
from contextlib import ExitStack

P = 128
D = 128
F = 27
SLOTS = 32
GROUP = 3 * SLOTS + F
Q = 4
CHUNKS = 5
X, Y, Z = 0, 7, 17
COPIES = [(0, F, X, CHUNKS), (1, F, X + CHUNKS, Y - X - CHUNKS),
          (2, F, Z, CHUNKS), (3, F, Z + CHUNKS, CHUNKS)]
OVER = [(0, Z, Y, CHUNKS), (1, Z, Y + CHUNKS, CHUNKS),
        (2, Y, X, CHUNKS), (3, Y, X + CHUNKS, Y - X - CHUNKS)]
WARM_UP = 11


def slot_order(looked):
    return [1 + k for k in looked] + [0] + [1 + k for k in range(F - 1) if k not in looked]


def place(low, high):
    if high < Y:
        n, row = 2 * CHUNKS + high - X, low
    elif high < Z:
        n, row = high - Y, low
    elif low < Y:
        n, row = low - X, high
    else:
        n, row = 2 * CHUNKS + high - Z, low
    return SLOTS * (n // CHUNKS) + row, n % CHUNKS


def dlrm_tower(nc, bottom, ids_rows, ids_cols, tables, looked, w_pair, w_bottom, b_top1, w_top2,
               b_top2, w_top3, out):
    f32, f32r, i32 = mybir.dt.float32, mybir.dt.float32r, mybir.dt.int32
    ALU, ACT = mybir.AluOpType, mybir.ActivationFunctionType

    B = bottom.shape[0] * bottom.shape[1]
    T = B // P
    gathered = [k for k in range(F - 1) if k not in looked]
    L, K = len(looked), len(gathered)
    VROWS = tables[looked[0]].shape[0] if L else 0
    CH = 8
    VP = VROWS // CH
    VP16 = VP // 16 * 16
    N1, N2 = b_top1.shape[1], b_top2.shape[1]
    NB = 4
    units = [list(range(a, min(a + NB, K))) for a in range(0, K, NB)]
    U = len(units)
    GH = 8
    PARTS = P // Q // GH
    MU = N1 + N2 + 1

    ctx = ExitStack()
    with ctx:
        def sb(name, shape, dt=f32):
            return ctx.enter_context(nc.sbuf_tensor(name, shape, dt))

        def pb(name, cols):
            return ctx.enter_context(nc.psum_tensor(name, [P, cols], f32))

        def sem(name):
            return ctx.enter_context(nc.semaphore(name))

        ids_g = sb("ids_g", [P, T, K], i32)
        ids_l = sb("ids_l", [P, L, B], i32)
        first_i = sb("first_i", [P, 1], i32)
        first_f = sb("first_f", [P, 1])
        ids_c = sb("ids_c", [P, 2, B], i32)
        raw = sb("raw", [VP, L, CH, D])
        high = sb("high", [VP, 2, CH, D], f32r)
        low = sb("low", [VP, 2, CH, D], f32r)
        hot = sb("hot", [VP, CH, B], f32r)
        bot = sb("bot", [P, T, D])
        bot_t = sb("bot_t", [D, B])
        emb = sb("emb", [P, 2, K, D])
        feat = sb("feat", [D, B, SLOTS])
        pairs = sb("pairs", [P, 2, CHUNKS, P])
        ident = sb("ident", [P, P])
        wp = sb("wp", [P, CHUNKS, N1, P])
        wb = sb("wb", [P, N1, P])
        w2 = sb("w2", [P, N1, N2, P])
        w3 = sb("w3", [P, N2])
        b1 = sb("b1", [P, N1])
        b2 = sb("b2", [P, N2])
        h1 = sb("h1", [P, N1, P])
        h2 = sb("h2", [P, N2, P])
        y = sb("y", [1, B])

        gram = [pb("gram0", GH * P), pb("gram1", GH * P)]
        turned = [pb("turned0", 512), pb("turned1", 512)]
        layer = [pb("layer0", 512), pb("layer1", 512)]

        ids_g_in = sem("ids_g_in")
        ids_l_in = [sem(f"ids_l_in{n}") for n in range(L)]
        bot_in = sem("bot_in")
        raw_in = [sem(f"raw_in{n}") for n in range(L)]
        w1_in = sem("w1_in")
        w2_in = sem("w2_in")
        emb_in = [[sem(f"emb_in{t}_{u}") for u in range(U)] for t in range(T)]
        zeroed = sem("zeroed")
        ident_ok = sem("ident_ok")
        first_ok = sem("first_ok")
        first_f_ok = sem("first_f_ok")
        ids_c_ok = sem("ids_c_ok")
        pads_ok = sem("pads_ok")
        high_ok = sem("high_ok")
        low_ok = sem("low_ok")
        hot_ok = sem("hot_ok")
        hot_used = sem("hot_used")
        turned_ok = sem("turned_ok")
        feat_act = sem("feat_act")
        feat_dve = sem("feat_dve")
        bot_t_ok = sem("bot_t_ok")
        gram_ok = sem("gram_ok")
        under_act = sem("under_act")
        under_dve = sem("under_dve")
        pairs_act = sem("pairs_act")
        pairs_dve = sem("pairs_dve")
        layer_ok = sem("layer_ok")
        layer_out = sem("layer_out")
        y_out = sem("y_out")

        fills = []
        for n in range(L):
            fills.append(("lookup", n))
            if n == 0:
                fills.append(("bottom",))
            if n >= L - U:
                fills.append(("turn", 0, n - (L - U)))
        head = len(fills)
        fills += [x for t in range(T) for u in range(U) if (x := ("turn", t, u)) not in fills]
        number = {x: n for n, x in enumerate(fills)}
        lookups = [n for n, x in enumerate(fills) if x[0] == "lookup"]
        turns_at = [n for n, x in enumerate(fills) if x[0] != "lookup"]

        def halves(n):
            return [slice(0, CH // 2), slice(CH // 2, CH)] if n == 0 else [slice(0, CH)]

        def halves_by(n):
            return n + 1 if n else 0

        def ring(n):
            same = lookups if fills[n][0] == "lookup" else turns_at
            return same, same.index(n)

        def bank(n):
            same, m = ring(n)
            return (layer if same is lookups else turned)[m % 2]

        def by_act(n):
            return n < head - 1 or (n >= head and ring(n)[1] % 2 == 0)

        def wait_feat(eng, n):
            act = sum(by_act(m) for m in range(n))
            eng.wait_ge(feat_act, act)
            if n > act:
                eng.wait_ge(feat_dve, n - act)

        def wait_bank(eng, n):
            same, m = ring(n)
            if m >= 2:
                before = same[m - 2]
                eng.wait_ge(feat_act if by_act(before) else feat_dve,
                            sum(by_act(k) == by_act(before) for k in range(before + 1)))

        def wait_turned(eng, n):
            same, m = ring(n)
            if same is lookups:
                eng.wait_ge(hot_used, CH * (m + 1))
            else:
                eng.wait_ge(turned_ok, m + 1)

        def move_fill(copy, n):
            what, *at = fills[n]
            src = bank(n)
            if what != "turn":
                slot = at[0] if what == "lookup" else L
                return copy(feat[:, :, slot], src[:, 0:B])
            t, u = at
            k = units[u]
            slots = slice(L + 1 + k[0], L + 2 + k[-1])
            return copy(feat[:, t * P:(t + 1) * P, slots],
                        src[:, 0:len(k) * P].rearrange("d (k b) -> d b k", b=P))

        def steps(t):
            turns = [("turn", t, u) for u in range(U) if number["turn", t, u] > head]
            products = [("multiply", t, part) for part in range(PARTS)]
            if t == 0:
                return [fills[head]] + products
            layers = [("dense", t - 1, m) for m in range(MU)]
            if t == T - 1:
                return (turns[:-2] + layers[:N1 - 1] + turns[-2:-1] + layers[N1 - 1:N1] + turns[-1:]
                        + layers[N1:N1 + 1] + products + layers[N1 + 1:])
            out, mixed = turns[:2], turns[2:]
            for i in range(N1 - 2):
                out += layers[i:i + 1] + mixed[i:i + 1]
            return (out + mixed[N1 - 2:] + layers[N1 - 2:N1 - 1] + products[:1] + layers[N1 - 1:N1]
                    + products[1:2] + layers[N1:MU - 1] + products[2:] + layers[MU - 1:])

        def move_pairs(eng, copy, t, part, samples, under, done):
            src = gram[part % 2][:].rearrange("p (g c) -> p c g", c=P)

            def to(s):
                return slice(Q * GH * part + s, Q * GH * (part + 1), Q)

            def move(s, q, rows, first, n):
                return copy(pairs[32 * q:32 * q + rows, t % 2, 0:n, to(s)],
                            src[32 * s:32 * s + rows, F * s + first:F * s + first + n])

            for s in samples:
                for quadrant in COPIES:
                    last = move(s, *quadrant)
                last.then_inc(under, 1)
            for i, s in enumerate(samples):
                eng.wait_ge(under, 2 * (PARTS * t + part) + i + 1)
                for quadrant in OVER:
                    last = move(s, *quadrant)
            last.then_inc(done, 1)

        ids_every = ids_cols.rearrange("(o l) b -> o l b", o=1).to_broadcast([P, L, B])

        block = ctx.enter_context(nc.Block())

        @block.sync
        def _(sp):
            sp.dma_start(ids_g[:], ids_rows).then_inc(ids_g_in, 16)
            for n, k in enumerate(looked):
                rows = tables[k].rearrange("(p c) d -> p c d", c=CH)
                sp.dma_start(raw[0:VP16, n], rows[0:VP16]).then_inc(raw_in[n], 16)
                sp.dma_start(raw[VP16:VP, n], rows[VP16:VP]).then_inc(raw_in[n], 16)
                if n + 1 < L:
                    sp.dma_start(ids_l[:, n + 1:n + 2], ids_every[:, n + 1:n + 2]).then_inc(ids_l_in[n + 1], 16)
                if n == 0:
                    sp.dma_start(bot[:], bottom.rearrange("t p d -> p t d")).then_inc(bot_in, 16)
            sp.wait_ge(hot_used, CH * max(L - 2, 1))
            sp.dma_start(wb[:], w_bottom.rearrange("p (n m) -> p n m", n=N1)).then_inc(w1_in, 16)
            sp.dma_start(wp[:], w_pair.rearrange("p j (n m) -> p j n m", n=N1)).then_inc(w1_in, 16)
            sp.dma_start(b1[:], b_top1).then_inc(w1_in, 16)
            sp.dma_start(w2[:], w_top2.rearrange("(k p) (n m) -> p k n m", p=P, n=N2)).then_inc(w2_in, 16)
            sp.dma_start(b2[:], b_top2).then_inc(w2_in, 16)
            sp.dma_start(w3[:], w_top3).then_inc(w2_in, 16)
            sp.wait_ge(layer_out, T * MU)
            sp.dma_start(out, y[:]).then_inc(y_out, 16)
            sp.wait_ge(y_out, 16)

        @block.gpsimd
        def _(pool):
            nc.gpsimd.memset(ident[:], 0.0).then_inc(zeroed, 1)
            nc.gpsimd.iota(first_i[:], [[1, 1]], base=0, channel_multiplier=-CH).then_inc(first_ok, 1)
            pool.wait_ge(zeroed, 1)
            nc.gpsimd.affine_select(out=ident[:], in_=ident[:], compare_op=ALU.not_equal, fill=1.0,
                                    base=0, pattern=[[-1, P]], channel_multiplier=1).then_inc(ident_ok, 1)
            pool.wait_ge(ids_g_in, 16)
            for t in range(T):
                for u, ks in enumerate(units):
                    if t >= 2:
                        wait_turned(pool, number["turn", t - 2, u])
                    for k in ks:
                        nc.gpsimd.indirect_dma_start(
                            out=emb[:, t % 2, k, :], out_offset=None, in_=tables[gathered[k]],
                            in_offset=bass.IndirectOffsetOnAxis(ap=ids_g[:, t, k:k + 1], axis=0),
                        ).then_inc(emb_in[t][u], 16)

        @block.vector
        def _(dve):
            copy = nc.vector.tensor_copy

            def spread(n):
                dve.wait_ge(ids_c_ok, n + 1)
                for c in range(CH):
                    if n >= 1:
                        dve.wait_ge(hot_used, CH * (n - 1) + c + 1)
                    nc.vector.tensor_single_scalar(hot[:, c], ids_c[0:VP, n % 2], c,
                                                   ALU.is_equal).then_inc(hot_ok, 1)
                    if c == 1:
                        if n >= 2:
                            dve.wait_ge(hot_used, CH * (n - 1))
                        for i, chunks in enumerate(halves(n)):
                            dve.wait_ge(high_ok, halves_by(n) + i + 1)
                            nc.vector.tensor_tensor(low[:, n % 2, chunks], raw[:, n, chunks],
                                                    high[:, n % 2, chunks].bitcast(f32),
                                                    ALU.subtract).then_inc(low_ok, 1)

            def fill(n):
                if not by_act(n):
                    wait_turned(dve, n)
                    move_fill(copy, n).then_inc(feat_dve, 1)

            dve.wait_ge(first_ok, 1)
            copy(first_f[:], first_i[:]).then_inc(first_f_ok, 1)
            nc.vector.memset(feat[:, :, F:SLOTS], 0.0)
            nc.vector.memset(pairs[:], 0.0).then_inc(pads_ok, 1)
            for n in range(L):
                spread(n)
            fill(head - 1)
            for t in range(T):
                for what, *at in steps(t):
                    if what == "turn":
                        fill(number["turn", *at])
                    elif what == "multiply":
                        t, part = at
                        dve.wait_ge(gram_ok, PARTS * t + part + 1)
                        if t >= 2 and part == 0:
                            dve.wait_ge(layer_ok, MU * (t - 2) + N1)
                        move_pairs(dve, copy, t, part, (2, 3), under_dve, pairs_dve)

        @block.scalar
        def _(act):
            copy = nc.scalar.copy

            def split(n):
                act.wait_ge(ids_l_in[n], 16)
                if n == 0:
                    act.wait_ge(first_f_ok, 1)
                if n >= 2:
                    act.wait_ge(hot_ok, CH * (n - 1))
                nc.scalar.activation(ids_c[:, n % 2], ids_l[:, n], ACT.Identity,
                                     bias=first_f[:, 0:1]).then_inc(ids_c_ok, 1)
                act.wait_ge(raw_in[n], 32)
                if n >= 2:
                    act.wait_ge(hot_used, CH * (n - 1))
                for chunks in halves(n):
                    copy(high[:, n % 2, chunks], raw[:, n, chunks]).then_inc(high_ok, 1)

            def fill(n):
                if by_act(n):
                    wait_turned(act, n)
                    if fills[n] == ("bottom",):
                        copy(bot_t[:], turned[0][:, 0:B]).then_inc(bot_t_ok, 1)
                    move_fill(copy, n).then_inc(feat_act, 1)

            def relu(t, m):
                act.wait_ge(layer_ok, MU * t + m + 1)
                src = layer[(MU * t + m) % 2]
                if m < N1:
                    if t == 0 and m == 0:
                        act.wait_ge(w1_in, 48)
                    ins = nc.scalar.activation(h1[:, m], src[:, 0:P], ACT.Relu, bias=b1[:, m:m + 1])
                elif m < N1 + N2:
                    if t == 0 and m == N1:
                        act.wait_ge(w2_in, 48)
                    n = m - N1
                    ins = nc.scalar.activation(h2[:, n], src[:, 0:P], ACT.Relu, bias=b2[:, n:n + 1])
                else:
                    ins = copy(y[0:1, t * P:(t + 1) * P], src[0:1, 0:P])
                ins.then_inc(layer_out, 1)

            act.dma_start(ids_l[:, 0:1], ids_every[:, 0:1]).then_inc(ids_l_in[0], 16)
            split(0)
            split(1)
            for n in range(head):
                fill(n)
                if fills[n][0] == "lookup" and fills[n][1] + 2 < L:
                    split(fills[n][1] + 2)
            for t in range(T):
                for what, *at in steps(t):
                    if what == "turn":
                        fill(number["turn", *at])
                    elif what == "dense":
                        relu(*at)
                    else:
                        t, part = at
                        act.wait_ge(gram_ok, PARTS * t + part + 1)
                        if t >= 2 and part == 0:
                            act.wait_ge(layer_ok, MU * (t - 2) + N1)
                        move_pairs(act, copy, t, part, (0, 1), under_act, pairs_act)
            for m in range(MU):
                relu(T - 1, m)

        @block.tensor
        def _(pe):
            groups = feat[:].rearrange("d (t g s) f -> d t g (s f)", t=T, s=Q)

            def lookup(n):
                m = number["lookup", n]
                wait_bank(pe, m)
                for c in range(CH):
                    part = c * len(halves(n)) // CH
                    pe.wait_ge(high_ok, halves_by(n) + part + 1)
                    pe.wait_ge(hot_ok, CH * n + c + 1)
                    nc.tensor.matmul(bank(m)[:, 0:B], high[:, n % 2, c], hot[:, c],
                                     start=(c == 0), stop=False)
                    pe.wait_ge(low_ok, halves_by(n) + part + 1)
                    nc.tensor.matmul(bank(m)[:, 0:B], low[:, n % 2, c], hot[:, c],
                                     start=False, stop=(c == CH - 1)).then_inc(hot_used, 1)

            def turn(t, u):
                n = number["turn", t, u]
                wait_bank(pe, n)
                pe.wait_ge(emb_in[t][u], 16 * len(units[u]))
                for i, k in enumerate(units[u]):
                    last = nc.tensor.transpose(bank(n)[:, i * P:(i + 1) * P], emb[:, t % 2, k], ident[:])
                last.then_inc(turned_ok, 1)

            def multiply(t, part):
                n = PARTS * t + part
                if n >= 2:
                    pe.wait_ge(pairs_act, n - 1)
                    pe.wait_ge(pairs_dve, n - 1)
                for i in range(GH):
                    g = GH * part + i
                    last = nc.tensor.matmul(gram[part % 2][0:GROUP, i * P:i * P + Q * F], groups[:, t, g, 0:GROUP],
                                            groups[:, t, g].rearrange("d (s f) -> d s f", s=Q)[:, :, 0:F],
                                            start=True, stop=True)
                last.then_inc(gram_ok, 1)

            def dense(t, m):
                n = MU * t + m
                if n >= 2:
                    pe.wait_ge(layer_out, n - 1)
                dst = layer[n % 2]
                if m < N1:
                    if m == 0:
                        if t == 0:
                            pe.wait_ge(w1_in, 48)
                            pe.wait_ge(bot_t_ok, 1)
                    nc.tensor.matmul(dst[:, 0:P], wb[:, m], bot_t[:, t * P:(t + 1) * P], start=True, stop=False)
                    if m == 0:
                        pe.wait_ge(pairs_act, PARTS * (t + 1))
                        pe.wait_ge(pairs_dve, PARTS * (t + 1))
                    for j in range(CHUNKS):
                        last = nc.tensor.matmul(dst[:, 0:P], wp[:, j, m], pairs[:, t % 2, j],
                                                start=False, stop=(j == CHUNKS - 1))
                elif m < N1 + N2:
                    if t == 0:
                        pe.wait_ge(w2_in, 48)
                    for k in range(N1):
                        pe.wait_ge(layer_out, MU * t + k + 1)
                        last = nc.tensor.matmul(dst[:, 0:P], w2[:, k, m - N1], h1[:, k],
                                                start=(k == 0), stop=(k == N1 - 1))
                else:
                    for k in range(N2):
                        pe.wait_ge(layer_out, MU * t + N1 + k + 1)
                        last = nc.tensor.matmul(dst[0:1, 0:P], w3[:, k:k + 1], h2[:, k],
                                                start=(k == 0), stop=(k == N2 - 1))
                last.then_inc(layer_ok, 1)

            pe.wait_ge(ident_ok, 1)
            for _ in range(WARM_UP):
                nc.tensor.matmul(gram[0][:, 0:P], ident[:], ident[:], start=True, stop=True)
            for what, *at in fills[:head]:
                if what == "lookup":
                    lookup(*at)
                elif what == "turn":
                    turn(*at)
                else:
                    pe.wait_ge(bot_in, 16)
                    for t in range(T):
                        last = nc.tensor.transpose(turned[0][:, t * P:(t + 1) * P], bot[:, t], ident[:])
                    last.then_inc(turned_ok, 1)
            pe.wait_ge(pads_ok, 1)
            for t in range(T):
                for what, *at in steps(t):
                    if what == "turn":
                        turn(*at)
                    elif what == "dense":
                        dense(*at)
                    else:
                        if at[1] == 0:
                            wait_feat(pe, max(head, number["turn", t, U - 1] + 1))
                        multiply(*at)
            for m in range(MU):
                dense(T - 1, m)


LOOKED = 7


def kernel(**inputs):
    import numpy as np
    import concourse.bacc as bacc
    from concourse.bass_utils import run_bass_kernel_spmd

    tables = [np.asarray(inputs[f"tbl_{k}"]) for k in range(F - 1)]
    least = min(t.shape[0] for t in tables)
    small = [k for k in range(F - 1) if tables[k].shape[0] == least and least % 8 == 0 and least <= 8 * P]
    looked = small[:LOOKED]
    order = slot_order(looked)

    ids = np.asarray(inputs["ids"])
    bottom = np.asarray(inputs["r_bottom_output"])
    B = ids.shape[0]
    T = B // P
    gathered = [k for k in range(F - 1) if k not in looked]
    ids_rows = ids[:, gathered].reshape(T, P, -1).transpose(1, 0, 2)
    ids_cols = ids[:, looked].T

    w1 = np.asarray(inputs["W_top1"])
    pair_rows = F * (F - 1) // 2
    w_pair = np.zeros((P, CHUNKS, w1.shape[1]), w1.dtype)
    at = {pair: n for n, pair in enumerate((i, j) for i in range(F) for j in range(i + 1, F))}
    for high in range(F):
        for low in range(high):
            w_pair[place(low, high)] = w1[at[tuple(sorted((order[low], order[high])))]]

    arrays = {
        "bottom": bottom.reshape(T, P, D),
        "ids_rows": ids_rows,
        "ids_cols": ids_cols,
        "w_pair": w_pair,
        "w_bottom": w1[pair_rows:],
        "b_top1": np.asarray(inputs["b_top1"]).reshape(-1, P).T,
        "w_top2": np.asarray(inputs["W_top2"]),
        "b_top2": np.asarray(inputs["b_top2"]).reshape(-1, P).T,
        "w_top3": np.asarray(inputs["W_top3"]).reshape(-1, P).T,
    }
    arrays |= {f"table{k}": t for k, t in enumerate(tables)}
    arrays = {n: np.ascontiguousarray(a) for n, a in arrays.items()}
    nc = bacc.Bacc("TRN2", target_bir_lowering=False, num_devices=1)
    aps = {n: nc.dram_tensor(n, a.shape, mybir.dt.from_np(a.dtype), kind="ExternalInput").ap()
           for n, a in arrays.items()}
    out = nc.dram_tensor("y_dram", (1, B), mybir.dt.float32, kind="ExternalOutput").ap()
    dlrm_tower(nc, aps["bottom"], aps["ids_rows"], aps["ids_cols"],
               [aps[f"table{k}"] for k in range(F - 1)], looked, aps["w_pair"], aps["w_bottom"],
               aps["b_top1"], aps["w_top2"], aps["b_top2"], aps["w_top3"], out)
    r = run_bass_kernel_spmd(nc, [arrays], core_ids=[0])
    return r.results[0]["y_dram"].reshape(B, 1)
```
